# Optimizing a Trainium2 kernel written in Bass

```python
import numpy as np
import jax
import jax.numpy as jnp

def _softmax(x, axis=-1):
    return jax.nn.softmax(x, axis=axis)

def _gelu(x):
    return jax.nn.gelu(x, approximate=True)

def _silu(x):
    return jax.nn.silu(x)

def _sigmoid(x):
    return jax.nn.sigmoid(x)

def _layernorm(x, axis=-1, eps=1e-05):
    m = jnp.mean(x, axis=axis, keepdims=True)
    v = jnp.var(x, axis=axis, keepdims=True)
    return (x - m) / jnp.sqrt(v + eps)

def _scatter_add(tgt, idx, src, axis=0):
    return tgt.at[idx].add(src)

def _segment_sum(src, seg, n):
    return jax.ops.segment_sum(src, seg, n)
kernel_name = 'mk_adj_seq_d1_adj_r2_d3fe24'

def setup_inputs(seed: int=0):
    np.random.seed(seed)
    _w = jnp.asarray

    def _rec_inputs():
        import jax
        import jax.numpy as jnp
        _gk = jax.random.key(seed)
        x = -0.000929 + 1 * jax.random.normal(jax.random.fold_in(_gk, 1), (4096, 128), jnp.float32)
        _a = jax.random.bernoulli(jax.random.fold_in(_gk, 2), 0.00390625, (4096, 4096))
        _a = jnp.logical_or(_a, jnp.swapaxes(_a, -1, -2))
        _a = jnp.logical_or(_a, jnp.eye(4096, dtype=bool))
        adj = _a.astype(jnp.int32)
        return (x, adj)
    x, adj = _rec_inputs()

    def _L0_gnn_setup():
        import jax, jax.numpy as jnp
        import numpy as np
        DIM = 128
        HEADS = 8
        DIM_FF = 512
        N = 2048
        HEAD_DIM = DIM // HEADS
        SCALE = HEAD_DIM ** (-0.5)

        def layer_norm(x, gamma, beta, eps=1e-05):
            mu = jnp.mean(x, axis=-1, keepdims=True)
            var = jnp.var(x, axis=-1, keepdims=True)
            return (x - mu) * jax.lax.rsqrt(var + eps) * gamma + beta
        key = jax.random.key(seed)
        ks = jax.random.split(key, 8)
        x = jax.random.normal(ks[0], (N, DIM), dtype=jnp.float32)
        adj = jax.random.randint(ks[1], (N, N), 0, 2, dtype=jnp.int32)
        adj = adj.at[jnp.arange(N), jnp.arange(N)].set(1)
        s = 1.0 / np.sqrt(DIM)
        w_qkv = jax.random.normal(ks[2], (DIM, 3 * DIM), dtype=jnp.float32) * s
        w_proj = jax.random.normal(ks[3], (DIM, DIM), dtype=jnp.float32) * s
        b_proj = jnp.zeros((DIM,), jnp.float32)
        w1 = jax.random.normal(ks[4], (DIM, DIM_FF), dtype=jnp.float32) * s
        b1 = jnp.zeros((DIM_FF,), jnp.float32)
        w2 = jax.random.normal(ks[5], (DIM_FF, DIM), dtype=jnp.float32) / np.sqrt(DIM_FF)
        b2 = jnp.zeros((DIM,), jnp.float32)
        g1 = jnp.ones((DIM,), jnp.float32)
        be1 = jnp.zeros((DIM,), jnp.float32)
        g2 = jnp.ones((DIM,), jnp.float32)
        be2 = jnp.zeros((DIM,), jnp.float32)
        return {'x': x, 'adj': adj, 'w_qkv': w_qkv, 'w_proj': w_proj, 'b_proj': b_proj, 'w1': w1, 'b1': b1, 'w2': w2, 'b2': b2, 'g1': g1, 'be1': be1, 'g2': g2, 'be2': be2}
    _L0_gnn_all = _L0_gnn_setup()
    _L0_gnn_in = {k: v for k, v in _L0_gnn_all.items() if k in ('w_qkv', 'w_proj', 'b_proj', 'w1', 'b1', 'w2', 'b2', 'g1', 'be1', 'g2', 'be2')}
    del _L0_gnn_all
    return {'x': x, 'adj': adj, 'L0_gnn_w_qkv': _L0_gnn_in['w_qkv'], 'L0_gnn_w_proj': _L0_gnn_in['w_proj'], 'L0_gnn_b_proj': _L0_gnn_in['b_proj'], 'L0_gnn_w1': _L0_gnn_in['w1'], 'L0_gnn_b1': _L0_gnn_in['b1'], 'L0_gnn_w2': _L0_gnn_in['w2'], 'L0_gnn_b2': _L0_gnn_in['b2'], 'L0_gnn_g1': _L0_gnn_in['g1'], 'L0_gnn_be1': _L0_gnn_in['be1'], 'L0_gnn_g2': _L0_gnn_in['g2'], 'L0_gnn_be2': _L0_gnn_in['be2']}

def reference(x, adj, L0_gnn_w_qkv, L0_gnn_w_proj, L0_gnn_b_proj, L0_gnn_w1, L0_gnn_b1, L0_gnn_w2, L0_gnn_b2, L0_gnn_g1, L0_gnn_be1, L0_gnn_g2, L0_gnn_be2):
    import jax
    import jax.numpy as jnp

    def _L0_gnn_ref(x, adj, w_qkv, w_proj, b_proj, w1, b1, w2, b2, g1, be1, g2, be2):
        import jax, jax.numpy as jnp
        import numpy as np
        DIM = 128
        HEADS = 8
        DIM_FF = 512
        N = 2048
        HEAD_DIM = DIM // HEADS
        SCALE = HEAD_DIM ** (-0.5)

        def layer_norm(x, gamma, beta, eps=1e-05):
            mu = jnp.mean(x, axis=-1, keepdims=True)
            var = jnp.var(x, axis=-1, keepdims=True)
            return (x - mu) * jax.lax.rsqrt(var + eps) * gamma + beta
        n = x.shape[0]
        qkv = layer_norm(x, g1, be1) @ w_qkv
        qkv = qkv.reshape(n, 3, HEADS, HEAD_DIM)
        q, k, v = (qkv[:, 0], qkv[:, 1], qkv[:, 2])
        scores = jnp.einsum('nhd,mhd->hnm', q, k) * SCALE
        mask = (adj != 0)[None, :, :]
        scores = jnp.where(mask, scores, -jnp.inf)
        attn = jax.nn.softmax(scores, axis=-1)
        out = jnp.einsum('hnm,mhd->nhd', attn, v).reshape(n, DIM)
        x = x + out @ w_proj + b_proj
        h2 = layer_norm(x, g2, be2)
        ff = jax.nn.gelu(h2 @ w1 + b1) @ w2 + b2
        return x + ff
    x = _L0_gnn_ref(x, adj, L0_gnn_w_qkv, L0_gnn_w_proj, L0_gnn_b_proj, L0_gnn_w1, L0_gnn_b1, L0_gnn_w2, L0_gnn_b2, L0_gnn_g1, L0_gnn_be1, L0_gnn_g2, L0_gnn_be2)
    return x

_drawn_inputs = setup_inputs


def setup_inputs(seed=0):
    import zlib

    import numpy as np

    out = dict(_drawn_inputs(seed))
    spreads = {'L0_gnn_b_proj': (0.0, 0.1),
     'L0_gnn_b1': (0.0, 0.1),
     'L0_gnn_b2': (0.0, 0.1),
     'L0_gnn_g1': (1.0, 0.2),
     'L0_gnn_be1': (0.0, 0.1),
     'L0_gnn_g2': (1.0, 0.2),
     'L0_gnn_be2': (0.0, 0.1)}
    factors = {}
    for name, (base, spread) in spreads.items():
        noise = np.random.default_rng([zlib.crc32(name.encode()), seed]).standard_normal(out[name].shape)
        drawn = base * np.exp(spread * noise) if base else spread * noise
        out[name] = jnp.asarray(drawn.astype(out[name].dtype))
    for name, factor in factors.items():
        out[name] = (out[name] * factor).astype(out[name].dtype)
    return out
```

```python
import numpy as np
import concourse.bass as bass
from concourse import mybir
from contextlib import ExitStack

F32 = mybir.dt.float32
BF16 = mybir.dt.bfloat16
FP8 = mybir.dt.float8e4
I32 = mybir.dt.int32
ALU = mybir.AluOpType
ACT = mybir.ActivationFunctionType
AX = mybir.AxisListType

N, DIM, HEADS, DIM_FF = 4096, 128, 8, 512
HD = DIM // HEADS
SCALE = HD ** -0.5
EPS = 1e-5
BIG = 2.0 ** 100
TILE = 512
TILES = N // TILE
SUB = TILE // 128
SUBS = N // 128
MB = N // 128
CHUNKS = N // 512
Q_PART = [0, 0, 1, 1, 0, 2]
K_PART = [0, 1, 0, 1, 2, 0]
STACK = HD * len(Q_PART)
KROWS = STACK + 3
PAIR = 2
HG = 2
GROUPS = HG * MB
EXPS = GROUPS * 2
ROWS = SUB * HEADS * CHUNKS
ROW_START, ROW_RATE = 3, 5
FC = DIM_FF // 128
ADJ_W = 1024
ADJ_C = N // ADJ_W

FILL_B = {1 + h: ("q", h) for h in range(HEADS)}
for _j, _steps in enumerate([(9, 10, 12, 14), (16, 19, 22, 25), (29, 34, 37, 40), (42, 46, 49, 52)]):
    FILL_B.update({g: ("mask", _j, f) for f, g in enumerate(_steps)})
for _j, _steps in enumerate([(17, 18), (31, 32), (44, 45), (57, 58)]):
    FILL_B.update({g: ("shift", _j, half) for half, g in enumerate(_steps)})
FILL_D = {11: ("sum", 0), 13: ("sum", 1), 15: ("proj",), 20: ("h2t",), 23: ("up", 0), 24: ("up", 1),
          26: ("up", 2), 27: ("up", 3), 33: ("down",)}
assert not set(FILL_B) & set(FILL_D)
NB, ND = len(FILL_B), len(FILL_D)
SQRT_STEP = 16
STORE_STEP = 36


def fills_before(i):
    if isinstance(i, int):
        return NB * min(i + 1, TILES) + ND * max(i - 1, 0)
    return i * (NB + ND) + (NB - ND)


def fill_plan(b, d):
    steps = {**(FILL_B if b else {}), **(FILL_D if d else {})}
    return {g: (n, steps[g]) for n, g in enumerate(sorted(steps))}


def row_units(g):
    first = ROW_RATE * (g - ROW_START)
    return range(max(first, 0), min(first + ROW_RATE, ROWS)) if g >= ROW_START else range(0)


def run_iterations(eng, body):
    body(-1, 1, True, False, False)
    body(0, 0, True, True, False)
    with eng.Fori(0, (TILES - 2) // 2) as pair:
        body(2 * pair + 1, 1, True, True, True)
        body(2 * pair + 2, 0, True, True, True)
    body(TILES - 1, 1, False, True, True)
    body(TILES, 0, False, False, True)


def program(nc, x, adj, w_qkv, w_proj, b_proj, w1, b1, w2, b2, g1, be1, g2, be2, const, out):
    with ExitStack() as ctx:
        def sb(name, shape, dt):
            return ctx.enter_context(nc.sbuf_tensor(name, shape, dt))

        def sem(name):
            return ctx.enter_context(nc.semaphore(name))

        xnT_dram = nc.dram_tensor("xnT_dram", (TILES, DIM, TILE), F32, kind="Internal").ap()

        k_stack = sb("k_stack", [KROWS, HEADS, N], BF16)
        q_stack = [sb(f"q_stack{p}", [KROWS, HEADS, TILE], BF16) for p in range(2)]
        v_ones = sb("v_ones", [128, MB, HEADS, HD + 1], F32)
        probs = sb("probs", [128, 4, PAIR * TILE], F32)
        mask_t = [sb(f"mask_t{p}", [128, MB, TILE], FP8) for p in range(2)]
        adj_in = sb("adj_in", [128, 2, ADJ_W], I32)
        row_mask = sb("row_mask", [128, 2, N], BF16)
        ident = sb("ident", [128, 128], F32)
        sum_sel = sb("sum_sel", [128, 128], F32)
        part_coef = sb("part_coef", [128, 4], F32)
        ident_bf = sb("ident_bf", [128, 128], BF16)
        neg_ident = sb("neg_ident", [128, 128], BF16)
        wqkv = sb("wqkv", [DIM, 3 * DIM], F32)
        wq_rep = sb("wq_rep", [DIM, HEADS, STACK], F32)
        wk_rep = sb("wk_rep", [DIM, HEADS, STACK], F32)
        w1_sb = sb("w1_sb", [DIM, DIM_FF], F32)
        w2_sb = sb("w2_sb", [128, FC, DIM], F32)
        wp_pad = sb("wp_pad", [128, HG, DIM], F32)
        b2_row = sb("b2_row", [1, DIM], F32)
        ones_row = sb("ones_row", [1, 128], F32)
        gb = sb("gb", [128, 4], F32)
        b1_col = sb("b1_col", [128, FC], F32)
        xq = sb("xq", [DIM, TILE], F32)
        q_hi = sb("q_hi", [STACK, TILE], BF16)
        q_rest = sb("q_rest", [STACK, TILE], F32)
        q_mid = sb("q_mid", [STACK, TILE], BF16)
        masked_out = sb("masked_out", [128, 2, 512], BF16)
        row_max = sb("row_max", [128, 2, HEADS, CHUNKS], F32)
        neg_max = sb("neg_max", [128, 2, HEADS], F32)
        max_part = sb("max_part", [128, 2, HEADS, 3], BF16)
        max_rest = sb("max_rest", [128, 2, HEADS], F32)
        attn = sb("attn", [128, HG, TILE], F32)
        recip = sb("recip", [128, TILE], F32)
        x_res = sb("x_res", [128, SUB, DIM], F32)
        rows2 = sb("rows2", [128, SUB, DIM], F32)
        h2T = sb("h2T", [128, TILE], F32)
        hidden = sb("hidden", [128, FC, TILE], F32)
        stats = sb("stats", [128, SUB, 6], F32)
        mean_var = sb("mean_var", [128, SUB, 2], F32)
        inv_var = sb("inv_var", [128, SUB], F32)
        rstd = sb("rstd", [128, SUB], F32)
        x_all = probs[:, :, :].rearrange("p a b -> p (a b)").rearrange("p (t d) -> p t d", d=DIM)
        xn_rows = [rows2[:, :, :], x_res[:, :, :]]
        xnT = [attn[:, p, :] for p in range(2)]
        k_hi = [hidden[0:STACK, 0, 256 * p:256 * p + 256].bitcast(BF16) for p in range(2)]
        k_mid = [hidden[0:STACK, 1, 256 * p:256 * p + 256].bitcast(BF16) for p in range(2)]
        k_rest = [hidden[0:STACK, 2 + p, :] for p in range(2)]

        score_ps = ctx.enter_context(nc.psum_tensor("score_ps", [128, 4, 512], F32))
        row_ps = ctx.enter_context(nc.psum_tensor("row_ps", [128, 2, 512], F32))
        pv_ps = ctx.enter_context(nc.psum_tensor("pv_ps", [128, 512], F32))
        aux_ps = ctx.enter_context(nc.psum_tensor("aux_ps", [128, 512], F32))
        aux_bf = aux_ps[:, :].bitcast(BF16)

        consts_in, x_first, x_in, w_in, wp_in = sem("consts_in"), sem("x_first"), sem("x_in"), sem("w_in"), sem("wp_in")
        wp_clear, set_up, k_ones, w_rep = sem("wp_clear"), sem("set_up"), sem("k_ones"), sem("w_rep")
        ln1_step, xt_full, xnT_ready, xnT_stored = sem("ln1_step"), sem("xt_full"), sem("xnT_ready"), sem("xnT_stored")
        v_full, v_done = sem("v_full"), sem("v_done")
        k_full, k_hi_done, k_rest_done, k_mid_done, k_done = (sem("k_full"), sem("k_hi_done"), sem("k_rest_done"),
                                                              sem("k_mid_done"), sem("k_done"))
        adj_loaded = [sem(f"adj_loaded{p}") for p in range(2)]
        mask_done, neg_max_done, split_step = sem("mask_done"), sem("neg_max_done"), sem("split_step")
        xq_loaded, q_hi_done, q_mid_done, q_done = sem("xq_loaded"), sem("q_hi_done"), sem("q_mid_done"), sem("q_done")
        row_full, row_done = sem("row_full"), sem("row_done")
        score_full, probs_done, pv_done, attn_ready = (sem("score_full"), sem("probs_done"), sem("pv_done"),
                                                       sem("attn_ready"))
        aux_full, aux_free = sem("aux_full"), sem("aux_free")
        rstd_done = sem("rstd_done")
        norm_done, x_res_in, ln2_step, out_stored = sem("norm_done"), sem("x_res_in"), sem("ln2_step"), sem("out_stored")

        passed = {e.engine: sem(f"passed_{n}") for n, e in (("pool", nc.gpsimd), ("act", nc.scalar), ("dve", nc.vector))}
        LN_STEPS = 3 * SUB + 2
        LN_STATS = 2 * SUB + 2

        def layer_norm_stats(wait_chain, chain, src):
            for s in range(SUB):
                nc.vector.bn_stats(stats[:, s, :], src[:, s, :]).then_inc(chain, 1)
            wait_chain(SUB)
            settled(nc.vector)
            for s in range(SUB):
                nc.vector.bn_aggr(mean_var[:, s, :], stats[:, s, :]).then_inc(chain, 1)
            wait_chain(2 * SUB)
            nc.vector.tensor_scalar(inv_var[:, :], mean_var[:, :, 1], EPS, None, ALU.add).then_inc(chain, 1)
            wait_chain(2 * SUB + 1)
            nc.vector.reciprocal(inv_var[:, :], inv_var[:, :]).then_inc(chain, 1)

        def layer_norm_apply(chain, src, dst):
            for s in range(SUB):
                nc.vector.tensor_scalar(dst[:, s, :], src[:, s, :], mean_var[:, s, 0:1], rstd[:, s:s + 1],
                                        ALU.subtract, ALU.mult).then_inc(chain, 1)

        def settled(eng):
            eng.sem_inc(passed[eng.engine], 1)

        block = ctx.enter_context(nc.Block())

        @block.sync
        def _(sp):
            x_view = x.rearrange("(t p) d -> p t d", p=128)
            sp.dma_start(x_all[:, 0:SUB, :], x_view[:, 0:SUB, :]).then_inc(x_first, 16)
            sp.dma_start(wqkv[:, :], w_qkv).then_inc(w_in, 16)
            sp.dma_start(ident[:, :], const[:, 0:128]).then_inc(consts_in, 16)
            sp.dma_start(sum_sel[:, :], const[:, 128:256]).then_inc(consts_in, 16)
            sp.dma_start(part_coef[:, :], const[:, 256:260]).then_inc(consts_in, 16)
            with nc.allow_non_contiguous_dma(reason="small vectors onto partitions"):
                for n, v in enumerate((g1, be1, g2, be2)):
                    sp.dma_start(gb[:, n:n + 1], v.rearrange("(p a) -> p a", a=1)).then_inc(consts_in, 16)
                sp.dma_start(b1_col[:, :], b1.rearrange("(f p) -> p f", p=128)).then_inc(consts_in, 16)
            sp.dma_start(x_all[:, SUB:, :], x_view[:, SUB:, :]).then_inc(x_in, 16)

            def load_adj(n, c):
                sp.dma_start(adj_in[:, c % 2, :], adj[bass.ts(n, 128), c * ADJ_W:(c + 1) * ADJ_W])\
                  .then_inc(adj_loaded[c % 2], 16)

            load_adj(0, 0)
            load_adj(0, 1)
            sp.dma_start(w1_sb[:, :], w1).then_inc(wp_in, 16)
            sp.dma_start(w2_sb[:, :, :], w2.rearrange("(f p) d -> p f d", p=128)).then_inc(wp_in, 16)
            sp.dma_start(b2_row[:, :], b2.rearrange("(a d) -> a d", a=1)).then_inc(wp_in, 16)
            sp.wait_ge(wp_clear, 1)
            for h in range(HEADS):
                r = 32 * (h % 4)
                sp.dma_start(wp_pad[r:r + HD, h // 4, :], w_proj[h * HD:(h + 1) * HD, :]).then_inc(wp_in, 16)
            sp.dma_start(wp_pad[HD:HD + 1, 0, :], b_proj.rearrange("(a d) -> a d", a=1)).then_inc(wp_in, 16)
            for c in range(2, ADJ_C):
                sp.wait_ge(mask_done, c - 1)
                load_adj(0, c)
            with sp.Fori(1, SUBS) as n:
                for c in range(ADJ_C):
                    sp.wait_ge(mask_done, n * ADJ_C + (c - 1))
                    load_adj(n, c)

        @block.gpsimd
        def _(pool):
            nc.gpsimd.memset(wp_pad[:, :, :], 0.0).then_inc(wp_clear, 1)
            nc.gpsimd.memset(ones_row[:, :], 1.0).then_inc(set_up, 1)
            nc.gpsimd.memset(v_ones[:, :, :, HD:HD + 1], 1.0).then_inc(k_ones, 1)
            pool.wait_ge(k_ones, 1)
            two_ones = float(np.array([0x3F803F80], np.uint32).view(np.float32)[0])
            nc.gpsimd.memset(k_stack[STACK:KROWS, :, :].rearrange("r h n -> r (h n)").bitcast(F32),
                             two_ones).then_inc(k_ones, 1)
            pool.wait_ge(k_ones, 2)

            def convert(n, slot, times):
                for c in range(ADJ_C):
                    pool.wait_ge(adj_loaded[c % 2], times * 16 + 16 * (c // 2 + 1))
                    settled(pool)
                    nc.gpsimd.tensor_scalar(row_mask[:, slot, c * ADJ_W:(c + 1) * ADJ_W], adj_in[:, c % 2, :],
                                            0.0, -BIG, ALU.is_equal, ALU.mult).then_inc(mask_done, 1)

            def split_max(n, slot):
                pool.wait_ge(neg_max_done, n + 1)
                settled(pool)
                full, rest, part = neg_max[:, slot, :], max_rest[:, slot, :], max_part[:, slot, :, :]
                nc.gpsimd.tensor_copy(part[:, :, 0], full).then_inc(split_step, 1)
                pool.wait_ge(split_step, n * 5 + 1)
                settled(pool)
                nc.gpsimd.tensor_tensor(rest, full, part[:, :, 0], ALU.subtract).then_inc(split_step, 1)
                pool.wait_ge(split_step, n * 5 + 2)
                settled(pool)
                nc.gpsimd.tensor_copy(part[:, :, 1], rest).then_inc(split_step, 1)
                pool.wait_ge(split_step, n * 5 + 3)
                settled(pool)
                nc.gpsimd.tensor_tensor(rest, rest, part[:, :, 1], ALU.subtract).then_inc(split_step, 1)
                pool.wait_ge(split_step, n * 5 + 4)
                settled(pool)
                nc.gpsimd.tensor_copy(part[:, :, 2], rest).then_inc(split_step, 1)

            convert(0, 0, 0)
            convert(1, 1, ADJ_C // 2)
            with pool.Fori(0, (SUBS - 2) // 2) as pair:
                n = 2 * pair
                for p in range(2):
                    split_max(n + p, p)
                    convert(n + (p + 2), p, n * (ADJ_C // 2) + (p + 2) * (ADJ_C // 2))
            split_max(SUBS - 2, 0)
            split_max(SUBS - 1, 1)

        @block.scalar
        def _(act):
            act.wait_ge(consts_in, 16 * 8)
            act.wait_ge(k_ones, 1)
            with act.Fori(0, TILES // 2) as cc:
                for p in range(2):
                    c0 = 2 * cc
                    c = 2 * cc + p
                    act.wait_ge(ln1_step, c * LN_STEPS + LN_STATS)
                    nc.scalar.activation(rstd[:, :], inv_var[:, :], ACT.Sqrt).then_inc(rstd_done, 1)
                    act.wait_ge(xt_full, c + 1)
                    if p == 0:
                        act.wait_ge(xnT_stored, c0 * 16)
                    nc.scalar.activation(xnT[p], row_ps[:, 0, :], ACT.Identity, scale=gb[:, 0:1],
                                         bias=gb[:, 1:2]).then_inc(xnT_ready, 1)
                    act.wait_ge(xnT_ready, c + 1)
                    act.dma_start(xnT_dram[bass.ds(c, 1), :, :].rearrange("a p n -> p (a n)"), xnT[p])\
                       .then_inc(xnT_stored, 16)
                    for h in range(HEADS + 1):
                        if h < HEADS:
                            act.wait_ge(k_full, c * 8 + (h + 1))
                            act.wait_ge(k_rest_done, c * 8 + max(h - 1, 0))
                            nc.scalar.copy(k_hi[h % 2], score_ps[0:STACK, h % 4, :]).then_inc(k_hi_done, 1)
                        if h >= 1:
                            act.wait_ge(k_rest_done, c * 8 + h)
                            act.wait_ge(k_done, c * 8 + max(h - 2, 0))
                            nc.scalar.copy(k_mid[(h - 1) % 2], k_rest[(h - 1) % 2]).then_inc(k_mid_done, 1)
                    act.wait_ge(v_full, c + 1)
                    nc.scalar.copy(v_ones[:, bass.ds(c * SUB, SUB), :, 0:HD],
                                   row_ps[:, 1, :].rearrange("p (s h d) -> p s h d", s=SUB, h=HEADS))\
                       .then_inc(v_done, 1)
            act.wait_ge(xnT_stored, 16 * TILES)

            x_view = x.rearrange("(t s p) d -> t p s d", p=128, s=SUB)
            out_view = out.rearrange("(t s p) d -> t p s d", p=128, s=SUB)

            def tile_of(view, t):
                return view[t] if isinstance(t, int) else view[bass.ds(t, 1)].rearrange("a p s d -> p (a s) d")

            def body(i, par, b, c, d):
                nxt = 1 - par
                base = fills_before(i)
                plan = fill_plan(b, d)
                for g in range(GROUPS):
                    if g == 0:
                        act.wait_ge(aux_free, base) if not (isinstance(i, int) and i < 0) else None
                        if b:
                            src = xnT_dram[i + 1] if isinstance(i, int) else \
                                xnT_dram[bass.ds(i + 1, 1)].rearrange("a p n -> p (a n)")
                            act.dma_start(xq[:, :], src).then_inc(xq_loaded, 16)
                        if d:
                            act.dma_start(x_res[:, :, :], tile_of(x_view, i - 1)).then_inc(x_res_in, 16)
                    if d and g == 1:
                        act.wait_ge(pv_done, i * GROUPS)
                        nc.scalar.copy(attn[:, 1, :], pv_ps[:, :]).then_inc(attn_ready, 1)
                    if c and g == MB + 1:
                        act.wait_ge(pv_done, i * GROUPS + MB)
                        nc.scalar.copy(attn[:, 0, :], pv_ps[:, :]).then_inc(attn_ready, 1)
                    if c:
                        for q in range(2):
                            n = 2 * g + q
                            act.wait_ge(score_full, i * EXPS + (n + 1))
                            if n >= 4 or not (isinstance(i, int) and i == 0):
                                act.wait_ge(pv_done, i * GROUPS + ((n - 4) // 2 + 1))
                            nc.scalar.activation(probs[:, n % 4, :],
                                                 score_ps[:, 2 * q:2 * q + 2, :].rearrange("p a n -> p (a n)"),
                                                 ACT.Exp).then_inc(probs_done, 1)
                    if b and 2 <= g <= HEADS + 1:
                        act.wait_ge(aux_free, base + plan[g - 1][0] + 1)
                        nc.scalar.copy(q_mid[:, :], q_rest[:, :]).then_inc(q_mid_done, 1)
                    if g in plan:
                        pos, what = plan[g]
                        if what[0] in ("q", "mask", "shift", "h2t", "up"):
                            act.wait_ge(aux_full, base + pos + 1)
                        if what[0] == "q":
                            nc.scalar.copy(q_hi[:, :], aux_ps[0:STACK, :]).then_inc(q_hi_done, 1)
                        elif what[0] == "mask":
                            _, j, f = what
                            settled(act)
                            nc.scalar.activation(mask_t[nxt][:, 8 * f:8 * f + 8, 128 * j:128 * (j + 1)],
                                                 aux_bf.rearrange("p (m n) -> p m n", m=8), ACT.Copy,
                                                 scale=-1.0 / BIG, saturate=False).then_inc(aux_free, 1)
                        elif what[0] == "shift":
                            _, j, half = what
                            nc.scalar.copy(q_stack[nxt][STACK:KROWS, 4 * half:4 * half + 4, 128 * j:128 * (j + 1)],
                                           aux_ps[STACK:KROWS, :].rearrange("p (h n) -> p h n", h=4))\
                               .then_inc(aux_free, 1)
                        elif what[0] == "h2t":
                            nc.scalar.activation(h2T[:, :], aux_ps[:, :], ACT.Identity, scale=gb[:, 2:3],
                                                 bias=gb[:, 3:4]).then_inc(aux_free, 1)
                        elif what[0] == "up":
                            f = what[1]
                            nc.scalar.activation(hidden[:, f, :], aux_ps[:, :], ACT.Gelu_apprx_tanh,
                                                 bias=b1_col[:, f:f + 1]).then_inc(aux_free, 1)
                    if d and g == SQRT_STEP:
                        act.wait_ge(ln2_step, (i - 1) * LN_STEPS + LN_STATS)
                        nc.scalar.activation(rstd[:, :], inv_var[:, :], ACT.Sqrt).then_inc(rstd_done, 1)
                    if d and g == STORE_STEP:
                        act.wait_ge(aux_free, base + plan[33][0] + 1)
                        act.dma_start(tile_of(out_view, i - 1), rows2[:, :, :]).then_inc(out_stored, 16)

            run_iterations(act, body)
            act.wait_ge(out_stored, 16 * TILES)

        @block.vector
        def _(dve):
            nc.vector.memset(pv_ps[:, :], 0.0).then_inc(set_up, 1)
            dve.wait_ge(w_in, 16)
            for r in range(len(Q_PART)):
                nc.vector.tensor_scalar(wq_rep[:, :, HD * r:HD * (r + 1)],
                                        wqkv[:, 0:DIM].rearrange("p (h d) -> p h d", d=HD), SCALE, None,
                                        ALU.mult).then_inc(w_rep, 1)
                nc.vector.tensor_copy(wk_rep[:, :, HD * r:HD * (r + 1)],
                                      wqkv[:, DIM:2 * DIM].rearrange("p (h d) -> p h d", d=HD)).then_inc(w_rep, 1)
            dve.wait_ge(consts_in, 16 * 8)
            nc.vector.tensor_copy(ident_bf[:, :], ident[:, :]).then_inc(w_rep, 1)
            nc.vector.tensor_scalar(neg_ident[:, :], ident[:, :], -BIG, None, ALU.mult).then_inc(w_rep, 1)
            dve.wait_ge(x_first, 16)
            with dve.Fori(0, TILES // 2) as cc:
                for p in range(2):
                    c0 = 2 * cc
                    c = 2 * cc + p
                    if p == 1:
                        dve.wait_ge(x_in, 16)

                    x_rows = x_all[:, bass.ds(c * SUB, SUB), :]
                    layer_norm_stats(lambda k: dve.wait_ge(ln1_step, c * LN_STEPS + k), ln1_step, x_rows)
                    dve.wait_ge(rstd_done, c + 1)
                    dve.wait_ge(xt_full, c0)
                    layer_norm_apply(ln1_step, x_rows, xn_rows[p])
                    for h in range(HEADS + 1):
                        if h < HEADS:
                            dve.wait_ge(k_hi_done, c * 8 + (h + 1))
                            dve.wait_ge(k_done, c * 8 + max(h - 1, 0))
                            nc.vector.scalar_tensor_tensor(k_rest[h % 2], k_hi[h % 2], part_coef[0:STACK, 2:3],
                                                           score_ps[0:STACK, h % 4, :], ALU.mult, ALU.add)\
                              .then_inc(k_rest_done, 1)
                        if h >= 1:
                            dve.wait_ge(k_mid_done, c * 8 + h)
                            nc.vector.scalar_tensor_tensor(k_stack[0:STACK, h - 1, bass.ds(c * 512, 512)],
                                                           k_mid[(h - 1) % 2], part_coef[0:STACK, 3:4],
                                                           k_rest[(h - 1) % 2], ALU.mult, ALU.add)\
                              .then_inc(k_done, 1)

            def body(i, par, b, c, d):
                nxt = 1 - par
                base = fills_before(i)
                plan = fill_plan(b, d)
                for g in range(GROUPS):
                    for u in row_units(g) if b else ():
                        j, h, ch = u // (HEADS * CHUNKS), u // CHUNKS % HEADS, u % CHUNKS
                        if h == 0 and ch == 0 and (j >= 2 or not (isinstance(i, int) and i == -1)):
                            dve.wait_ge(neg_max_done, (i + 1) * SUB + (j - 1))
                        dve.wait_ge(row_full, (i + 1) * ROWS + (u + 1))
                        if h == 0 and ch % 2 == 0:
                            dve.wait_ge(mask_done, (i + 1) * (SUB * ADJ_C) + (j * ADJ_C + ch // 2 + 1))
                        settled(dve)
                        nc.vector.tensor_tensor_reduce(
                            out=masked_out[:, u % 2, :], in0=row_ps[:, u % 2, :],
                            in1=row_mask[:, j % 2, ch * 512:(ch + 1) * 512], scale=1.0, scalar=-3.0e38,
                            op0=ALU.add, op1=ALU.max, accum_out=row_max[:, j % 2, h, ch:ch + 1]).then_inc(row_done, 1)
                        if u % (HEADS * CHUNKS) == HEADS * CHUNKS - 1:
                            if j >= 2 or not (isinstance(i, int) and i == -1):
                                dve.wait_ge(split_step, (i + 1) * (5 * SUB) + 5 * (j - 1))
                            dve.wait_ge(row_done, (i + 1) * ROWS + (u + 1))
                            nc.vector.tensor_reduce(neg_max[:, j % 2, :], row_max[:, j % 2, :, :], AX.X, ALU.max,
                                                    negate=True).then_inc(neg_max_done, 1)
                    if b and 2 <= g <= HEADS + 1:
                        h = g - 2
                        dve.wait_ge(q_mid_done, (i + 1) * HEADS + (h + 1))
                        if h == 0 and c and not (isinstance(i, int) and i == 0):
                            dve.wait_ge(probs_done, i * EXPS)
                        nc.vector.scalar_tensor_tensor(q_stack[nxt][0:STACK, h, :], q_mid[:, :],
                                                       part_coef[0:STACK, 1:2], q_rest[:, :], ALU.mult,
                                                       ALU.add).then_inc(q_done, 1)
                    if d and g == SQRT_STEP + 1:
                        dve.wait_ge(rstd_done, TILES + i)
                        if not (isinstance(i, int) and i == 1):
                            dve.wait_ge(out_stored, (i - 1) * 16)
                        layer_norm_apply(ln2_step, x_res, rows2)
                    if g not in plan:
                        continue
                    pos, what = plan[g]
                    if what[0] == "q":
                        dve.wait_ge(q_hi_done, (i + 1) * HEADS + (what[1] + 1))
                        dve.wait_ge(q_done, (i + 1) * HEADS + what[1])
                        nc.vector.scalar_tensor_tensor(q_rest[:, :], q_hi[:, :], part_coef[0:STACK, 0:1],
                                                       aux_ps[0:STACK, :], ALU.mult, ALU.add).then_inc(aux_free, 1)
                    elif what[0] == "sum":
                        hg = what[1]
                        dve.wait_ge(norm_done, (i - 1) * HG + hg)
                        dve.wait_ge(aux_full, base + pos + 1)
                        nc.vector.reciprocal(recip[:, :], aux_ps[:, :]).then_inc(aux_free, 1)
                        dve.wait_ge(aux_free, base + pos + 1)
                        nc.vector.tensor_tensor(attn[:, hg, :], attn[:, hg, :], recip[:, :], ALU.mult)\
                          .then_inc(norm_done, 1)
                    elif what[0] == "proj":
                        dve.wait_ge(aux_full, base + pos + 1)
                        dve.wait_ge(x_res_in, i * 16)
                        nc.vector.tensor_tensor(x_res[:, :, :].rearrange("p s d -> p (s d)"), aux_ps[:, :],
                                                x_res[:, :, :].rearrange("p s d -> p (s d)"), ALU.add)\
                          .then_inc(aux_free, 1)
                        dve.wait_ge(aux_free, base + pos + 1)

                        layer_norm_stats(lambda k: dve.wait_ge(ln2_step, (i - 1) * LN_STEPS + k), ln2_step, x_res)
                    elif what[0] == "down":
                        dve.wait_ge(aux_full, base + pos + 1)
                        nc.vector.tensor_tensor(rows2[:, :, :].rearrange("p s d -> p (s d)"), aux_ps[:, :],
                                                x_res[:, :, :].rearrange("p s d -> p (s d)"), ALU.add)\
                          .then_inc(aux_free, 1)

            run_iterations(dve, body)

        @block.tensor
        def _(pe):
            pe.wait_ge(consts_in, 16 * 8)
            pe.wait_ge(w_rep, 2 * len(Q_PART) + 2)
            pe.wait_ge(set_up, 2)
            with pe.Fori(0, TILES // 2) as cc:
                for p in range(2):
                    c0 = 2 * cc
                    c = 2 * cc + p
                    pe.wait_ge(ln1_step, c * LN_STEPS + LN_STEPS)
                    for s in range(SUB):
                        last = nc.tensor.transpose(row_ps[:, 0, 128 * s:128 * (s + 1)], xn_rows[p][:, s, :], ident[:, :])
                    last.then_inc(xt_full, 1)
                    pe.wait_ge(xnT_ready, c + 1)
                    for h in range(HEADS):
                        if h >= 4:
                            pe.wait_ge(k_rest_done, c * 8 + (h - 3))
                        elif p == 1:
                            pe.wait_ge(k_rest_done, c * 8 + (h - 3))
                        else:
                            pe.wait_ge(k_rest_done, c0 * 8)
                        nc.tensor.matmul(score_ps[0:STACK, h % 4, :], wk_rep[:, h, :], xnT[p], start=True,
                                         stop=True).then_inc(k_full, 1)
                    pe.wait_ge(v_done, c)
                    for s in range(SUB):
                        last = nc.tensor.matmul(row_ps[:, 1, 128 * s:128 * (s + 1)], xnT[p][:, 128 * s:128 * (s + 1)],
                                                wqkv[:, 2 * DIM:3 * DIM], start=True, stop=True)
                    last.then_inc(v_full, 1)
            pe.wait_ge(k_done, HEADS * TILES)
            pe.wait_ge(k_ones, 2)
            pe.wait_ge(v_done, TILES)
            pe.wait_ge(wp_in, 16 * (3 + HEADS + 1))

            def row_scores(i, nxt, u):
                j, h, ch = u // (HEADS * CHUNKS), u // CHUNKS % HEADS, u % CHUNKS
                if j == 0 and ch == 0:
                    pe.wait_ge(q_done, (i + 1) * HEADS + (h + 1))
                if u >= 2 or not (isinstance(i, int) and i == -1):
                    pe.wait_ge(row_done, (i + 1) * ROWS + (u - 1))
                nc.tensor.matmul(row_ps[:, u % 2, :], q_stack[nxt][0:STACK, h, 128 * j:128 * (j + 1)],
                                 k_stack[0:STACK, h, ch * 512:(ch + 1) * 512], start=True, stop=True)\
                  .then_inc(row_full, 1)

            def pair_scores(i, par, g, q):
                hg, m = g // MB, g % MB
                n = 2 * g + q
                if n >= 2 or not (isinstance(i, int) and i == 0):
                    pe.wait_ge(probs_done, i * EXPS + (n - 1))
                for a in range(PAIR):
                    h = 4 * hg + PAIR * q + a
                    nc.tensor.matmul(score_ps[:, 2 * q + a, :], k_stack[:, h, 128 * m:128 * (m + 1)],
                                     q_stack[par][:, h, :], start=True, stop=False)
                for a in range(PAIR):
                    last = nc.tensor.matmul(score_ps[:, 2 * q + a, :], neg_ident[:, :], mask_t[par][:, m, :],
                                            start=False, stop=True)
                last.then_inc(score_full, 1)

            def weigh_values(i, g):
                hg, m = g // MB, g % MB
                pe.wait_ge(probs_done, i * EXPS + (2 * g + 2))
                if m == 0 and not (isinstance(i, int) and i == 0 and hg == 0):
                    pe.wait_ge(attn_ready, i * HG + hg)
                for k in range(4):
                    n = 2 * g + k // PAIR
                    last = nc.tensor.matmul(pv_ps[32 * k:32 * k + HD + 1, :], v_ones[:, m, 4 * hg + k, :],
                                            probs[:, n % 4, (k % PAIR) * TILE:(k % PAIR + 1) * TILE],
                                            start=(m == 0), stop=(m == MB - 1))
                last.then_inc(pv_done, 1)

            def fill(i, nxt, base, pos, what):
                if pos > 0 or not (isinstance(i, int) and i == -1):
                    pe.wait_ge(aux_free, base + pos)
                if what[0] == "q":
                    if what[1] == 0:
                        pe.wait_ge(xq_loaded, (i + 2) * 16)
                    last = nc.tensor.matmul(aux_ps[0:STACK, :], wq_rep[:, what[1], :], xq[:, :], start=True, stop=True)
                elif what[0] == "mask":
                    _, j, f = what
                    pe.wait_ge(mask_done, (i + 1) * (SUB * ADJ_C) + (j * ADJ_C + f + 1))
                    for m in range(8):
                        last = nc.tensor.transpose(aux_bf[:, 128 * m:128 * (m + 1)],
                                                   row_mask[:, j % 2, (8 * f + m) * 128:(8 * f + m + 1) * 128],
                                                   ident_bf[:, :])
                elif what[0] == "shift":
                    _, j, half = what
                    pe.wait_ge(split_step, (i + 1) * (5 * SUB) + 5 * (j + 1))
                    for k in range(4):
                        last = nc.tensor.matmul(aux_ps[STACK:KROWS, 128 * k:128 * (k + 1)],
                                                max_part[:, j % 2, 4 * half + k, :], ident_bf[:, :],
                                                start=True, stop=True)
                elif what[0] == "sum":
                    pe.wait_ge(attn_ready, (i - 1) * HG + (what[1] + 1))
                    last = nc.tensor.matmul(aux_ps[:, :], sum_sel[:, :], attn[:, what[1], :], start=True, stop=True)
                elif what[0] == "proj":
                    pe.wait_ge(norm_done, i * HG)
                    for s in range(SUB):
                        for hg in range(HG):
                            last = nc.tensor.matmul(aux_ps[:, 128 * s:128 * (s + 1)], attn[:, hg, 128 * s:128 * (s + 1)],
                                                    wp_pad[:, hg, :], start=(hg == 0), stop=(hg == HG - 1))
                elif what[0] == "h2t":
                    pe.wait_ge(ln2_step, i * LN_STEPS)
                    for s in range(SUB):
                        last = nc.tensor.transpose(aux_ps[:, 128 * s:128 * (s + 1)], rows2[:, s, :], ident[:, :])
                elif what[0] == "up":
                    f = what[1]
                    last = nc.tensor.matmul(aux_ps[:, :], w1_sb[:, 128 * f:128 * (f + 1)], h2T[:, :], start=True, stop=True)
                elif what[0] == "down":
                    for s in range(SUB):
                        for f in range(FC):
                            nc.tensor.matmul(aux_ps[:, 128 * s:128 * (s + 1)], hidden[:, f, 128 * s:128 * (s + 1)],
                                             w2_sb[:, f, :], start=(f == 0), stop=False)
                        last = nc.tensor.matmul(aux_ps[:, 128 * s:128 * (s + 1)], ones_row[:, :], b2_row[:, :],
                                                start=False, stop=True)
                last.then_inc(aux_full, 1)

            def body(i, par, b, c, d):
                nxt = 1 - par
                base = fills_before(i)
                plan = fill_plan(b, d)
                if c:
                    pe.wait_ge(aux_free, base)
                for g in range(GROUPS):
                    rows = list(row_units(g)) if b else []
                    if c:
                        pair_scores(i, par, g, 0)
                    for u in rows[0:2]:
                        row_scores(i, nxt, u)
                    if c:
                        pair_scores(i, par, g, 1)
                    for u in rows[2:4]:
                        row_scores(i, nxt, u)
                    if g == 0 and d:
                        weigh_values(i - 1, GROUPS - 1)
                    if g > 0 and c:
                        weigh_values(i, g - 1)
                    for u in rows[4:]:
                        row_scores(i, nxt, u)
                    if g in plan:
                        fill(i, nxt, base, *plan[g])

            run_iterations(pe, body)


def constants():
    c = np.zeros((128, 260), np.float32)
    c[:, 0:128] = np.eye(128)
    for col in range(128):
        c[32 * (col // 32) + HD, 128 + col] = 1.0
    for r in range(STACK):
        c[r, 256] = -1.0 if Q_PART[r // HD] >= 1 else 0.0
        c[r, 257] = -1.0 if Q_PART[r // HD] == 2 else 0.0
        c[r, 258] = -1.0 if K_PART[r // HD] >= 1 else 0.0
        c[r, 259] = -1.0 if K_PART[r // HD] == 2 else 0.0
    return c


def kernel(**inputs):
    import concourse.bacc as bacc
    from concourse.bass_utils import run_bass_kernel_spmd

    nc = bacc.Bacc("TRN2", target_bir_lowering=False, num_devices=1, dynamic_dma_scratch_size=1024)
    names = ["x", "adj"] + ["L0_gnn_" + n for n in
                            ("w_qkv", "w_proj", "b_proj", "w1", "b1", "w2", "b2", "g1", "be1", "g2", "be2")]
    arrays = {n: np.ascontiguousarray(inputs[n]) for n in names}
    arrays["const"] = constants()
    args = [nc.dram_tensor(n, a.shape, mybir.dt.from_np(a.dtype), kind="ExternalInput").ap()
            for n, a in arrays.items()]
    out = nc.dram_tensor("out", (N, DIM), F32, kind="ExternalOutput").ap()
    program(nc, *args, out)
    result = run_bass_kernel_spmd(nc, [arrays], core_ids=[0])
    return result.results[0]["out"]
```

```python
import numpy as np
import concourse.bass as bass
from concourse import mybir
from contextlib import ExitStack

F32 = mybir.dt.float32
BF16 = mybir.dt.bfloat16
FP8 = mybir.dt.float8e4
I32 = mybir.dt.int32
ALU = mybir.AluOpType
ACT = mybir.ActivationFunctionType
AX = mybir.AxisListType

N, DIM, HEADS, DIM_FF = 4096, 128, 8, 512
HD = DIM // HEADS
SCALE = HD ** -0.5
EPS = 1e-5
BIG = 2.0 ** 100
TILE = 512
TILES = N // TILE
SUB = TILE // 128
SUBS = N // 128
MB = N // 128
CHUNKS = N // 512
Q_PART = [0, 0, 1, 1, 0, 2]
K_PART = [0, 1, 0, 1, 2, 0]
STACK = HD * len(Q_PART)
KROWS = STACK + 3
PAIR = 2
HG = 2
GROUPS = HG * MB
EXPS = GROUPS * 2
ROWS = SUB * HEADS * CHUNKS
SPLIT_OPS = 5
LAG = 2
SLOTS = 7
FC = DIM_FF // 128
ROW_START, ROW_END = 3, 60
POOL_MASK = (7,11,15,19,23)
ROW_LESS = {**{g: 3 for g in range(3, 10)}, **{g: 3 for m in POOL_MASK for g in (m, m + MB)}, 11: 0, 12: 3, 13: 0, 38: 0}
ADJ_W = 1024
ADJ_C = N // ADJ_W

FILL_B = {h: ("q", h) for h in range(HEADS)}
for _j, _steps in enumerate([(9, 13, 16, 17), (22, 26, 27, 29), (30, 31, 34, 36), (40, 41, 44, 45)]):
    FILL_B.update({g: ("mask", _j, f) for f, g in enumerate(_steps)})
FILL_B.update({g: ("shift", _j) for _j, g in enumerate([33, 38, 52, 62])})
FILL_C = {37: ("sum", 0)}
FILL_D = {10: ("sum", 1), 12: ("proj",), 18: ("h2t",), 20: ("up", 0), 21: ("up", 1), 24: ("up", 2), 25: ("up", 3),
          32: ("down",)}
CONVERT = {}
for _j, _steps in enumerate([(0, 1, 2, 3), (21, 22, 25, 27), (33, 34, 35, 36), (49, 50, 53, 54)]):
    CONVERT.update({g: (_j + 1, f) for f, g in enumerate(_steps)})
SPLIT = {21: 0, 33: 1, 47: 2, 60: 3}
assert len({**FILL_B, **FILL_C, **FILL_D}) == len(FILL_B) + len(FILL_C) + len(FILL_D)
NB, ND = len(FILL_B), len(FILL_C) + len(FILL_D)
XQ_STEP = 40
SQRT_STEP = 14
GELU_STEP = 28
STORE_STEP = 36
SEEN_STEP = 50

ITEMS = HEADS * (1 + CHUNKS)
DEPTH = 4
ROW_LAG = 4
FIRST_STEPS = ITEMS + ROW_LAG
FIRST_FILLS = ADJ_C * SUB
FIRST_MASKS = {18 + 3 * n: n for n in range(FIRST_FILLS)}
DVE_MASKS = {3: 2, 5: 3}
POOL_FIRST_MASKS = {10 + 4 * k: 4 + k for k in range(FIRST_FILLS - 4)}
POOL_NEXT_MASKS = {60: 0, 64: 1, 68: 2}
POOL_ONES = {11 + 8 * h: h for h in range(HEADS)}


def first_rows(st):
    n = st - ROW_LAG
    return (n % HEADS, n // HEADS - 1) if n >= HEADS else (None, None)


def fills_before(i):
    if isinstance(i, int):
        if i == 0:
            return FIRST_FILLS
        return FIRST_FILLS + NB * min(i, TILES - 1) + len(FILL_C) * i + len(FILL_D) * (i - 1)
    return i * (NB + ND) + (FIRST_FILLS - len(FILL_D))


def fill_plan(b, c, d):
    steps = {**(FILL_B if b else {}), **(FILL_C if c else {}), **(FILL_D if d else {})}
    return {g: (n, steps[g]) for n, g in enumerate(sorted(steps))}


def pool_masked(m):
    return m in POOL_MASK


POOL_PAIRS = {}
for _g in range(GROUPS):
    if pool_masked(_g % MB):
        for _q in range(2):
            POOL_PAIRS[_g, _q] = len(POOL_PAIRS)
NP = len(POOL_PAIRS)
OTHER_PAIRS = {}
for _g in range(GROUPS):
    if not pool_masked(_g % MB):
        for _q in range(2):
            OTHER_PAIRS[_g, _q] = len(OTHER_PAIRS)
NO = len(OTHER_PAIRS)
assert not pool_masked(MB - 1) and not pool_masked(0)


def row_units(g):
    free = [k for k in range(ROW_START, ROW_END) if k not in ROW_LESS]
    spread = ROWS - sum(ROW_LESS.values())
    first = sum(n for k, n in ROW_LESS.items() if k < g) + spread * sum(k < g for k in free) // len(free)
    if g in ROW_LESS:
        return list(range(first, first + ROW_LESS[g]))
    if g not in free:
        return []
    return list(range(first, first + spread * (free.index(g) + 1) // len(free) - spread * free.index(g) // len(free)))


TURNS_OF_6 = next(n for n in range(0, EXPS, 6) if (EXPS - n) % 7 == 0)
PLACE = [n % 6 if n < TURNS_OF_6 else (n - TURNS_OF_6) % 7 for n in range(EXPS)]


def slot(g, q):
    return PLACE[2 * g + q]


def last_user(g, q):
    n = 2 * g + q
    return next(k for k in range(n - 1, n - EXPS, -1) if PLACE[k] == PLACE[n]) // 2


def run_iterations(eng, body, pairs=(TILES - 2) // 2):
    body(0, 0, True, True, False)
    with eng.Fori(0, pairs) as pair:
        body(2 * pair + 1, 1, True, True, True)
        body(2 * pair + 2, 0, True, True, True)
    for i in range(2 * pairs + 1, TILES - 1):
        body(i, i % 2, True, True, True)
    body(TILES - 1, 1, False, True, True)
    body(TILES, 0, False, False, True)


def program(nc, x, adj, w_qkv, w_proj, b_proj, w1, b1, w2, b2, g1, be1, g2, be2, const, out):
    with ExitStack() as ctx:
        def sb(name, shape, dt):
            return ctx.enter_context(nc.sbuf_tensor(name, shape, dt))

        def sem(name):
            return ctx.enter_context(nc.semaphore(name))

        xnT_dram = nc.dram_tensor("xnT_dram", (TILES + 1, DIM, TILE), F32, kind="Internal").ap()

        k_stack = sb("k_stack", [KROWS, HEADS, N], BF16)
        q_stack = [sb(f"q_stack{p}", [KROWS, HEADS, TILE], BF16) for p in range(2)]
        v_ones = sb("v_ones", [128, MB, HEADS, HD + 1], F32)
        probs = sb("probs", [128, SLOTS, PAIR * TILE], F32)
        mask_t = [sb(f"mask_t{p}", [128, MB, TILE], FP8) for p in range(2)]
        adj_in = sb("adj_in", [128, 2, ADJ_W], I32)
        row_mask = sb("row_mask", [128, 2, N], BF16)
        ident = sb("ident", [128, 128], F32)
        sum_sel = sb("sum_sel", [128, 128], F32)
        part_coef = sb("part_coef", [128, 4], F32)
        ident_bf = sb("ident_bf", [128, 128], BF16)
        neg_ident = sb("neg_ident", [128, 128], BF16)
        wq_rep = sb("wq_rep", [DIM, HEADS, STACK], F32)
        w1_sb = sb("w1_sb", [DIM, DIM_FF], F32)
        w2_sb = sb("w2_sb", [128, FC, DIM], F32)
        wp_pad = sb("wp_pad", [128, HG, DIM], F32)
        b2_row = sb("b2_row", [1, DIM], F32)
        ones_row = sb("ones_row", [1, 128], F32)
        gb = sb("gb", [128, 4], F32)
        b1_col = sb("b1_col", [128, FC], F32)
        xq = sb("xq", [DIM, TILE], F32)
        q_hi = sb("q_hi", [STACK, TILE], BF16)
        q_rest = sb("q_rest", [STACK, TILE], F32)
        q_mid = sb("q_mid", [STACK, TILE], BF16)
        masked_out = sb("masked_out", [128, 2, 512], BF16)
        row_max = sb("row_max", [128, SUB, HEADS, CHUNKS], F32)
        neg_max = sb("neg_max", [128, SUB, HEADS], F32)
        max_part = sb("max_part", [128, SUB, HEADS, 3], BF16)
        max_rest = sb("max_rest", [128, SUB, HEADS], F32)
        attn = sb("attn", [128, HG, TILE], F32)
        recip = sb("recip", [128, TILE], F32)
        x_res = sb("x_res", [128, SUB, DIM], F32)
        rows2 = sb("rows2", [128, SUB, DIM], F32)
        h2T = sb("h2T", [128, TILE], F32)
        hidden = sb("hidden", [128, FC, TILE], F32)
        stats = sb("stats", [128, SUB, 6], F32)
        mean_var = sb("mean_var", [128, SUB, 2], F32)
        inv_var = sb("inv_var", [128, SUB], F32)
        rstd = sb("rstd", [128, SUB], F32)
        x_all = probs[:, 0:4, :].rearrange("p a b -> p (a b)").rearrange("p (t d) -> p t d", d=DIM)
        wk_rep = probs[:, 4, 0:HEADS * STACK].rearrange("p (h r) -> p h r", r=STACK)
        wqkv = probs[:, 5, 0:3 * DIM]
        xn_rows = [rows2[:, :, :], x_res[:, :, :]]
        xnT = [attn[:, p, :] for p in range(2)]
        item_hi = [hidden[0:STACK, 0, 256 * p:256 * p + 256].bitcast(BF16) for p in range(2)]
        item_mid = [view[0:STACK, 256 * p:256 * p + 256].bitcast(BF16) for view in (hidden[:, 1, :], h2T) for p in range(2)]
        item_rest = [hidden[0:STACK, 2, :], hidden[0:STACK, 3, :],
                     probs[0:STACK, 6, 0:TILE], probs[0:STACK, 6, TILE:2 * TILE]]
        late_mask = mask_t[1][:, :, :].rearrange("p m n -> p (m n)").bitcast(BF16).rearrange("p (a n) -> p a n", a=2)
        first_mask = [row_mask[:, 0, :], row_mask[:, 1, :], late_mask[:, 0, :], late_mask[:, 1, :]]

        score_ps = ctx.enter_context(nc.psum_tensor("score_ps", [128, 4, 512], F32))
        row_ps = ctx.enter_context(nc.psum_tensor("row_ps", [128, 2, 512], F32))
        pv_ps = ctx.enter_context(nc.psum_tensor("pv_ps", [128, 512], F32))
        aux_ps = ctx.enter_context(nc.psum_tensor("aux_ps", [128, 512], F32))
        aux_bf = aux_ps[:, :].bitcast(BF16)

        consts_in, x_first, x_in, w_in, wp_in = sem("consts_in"), sem("x_first"), sem("x_in"), sem("w_in"), sem("wp_in")
        wp_clear, set_up, k_ones, w_rep = sem("wp_clear"), sem("set_up"), sem("k_ones"), sem("w_rep")
        ln1_step, xnT_ready, xnT_stored = sem("ln1_step"), sem("xnT_ready"), [sem(f"xnT_stored{p}") for p in range(2)]
        stage_full, v_done = sem("stage_full"), sem("v_done")
        item_full, hi_done, rest_done, mid_done, item_done = (sem("item_full"), sem("hi_done"), sem("rest_done"),
                                                              sem("mid_done"), sem("item_done"))
        shift_full, shift_stored = sem("shift_full"), sem("shift_stored")
        scores_bounded, exps_bounded = sem("scores_bounded"), sem("exps_bounded")
        probs_masked, gelu_done, pv_clear = sem("probs_masked"), sem("gelu_done"), sem("pv_clear")
        adj_loaded = [sem(f"adj_loaded{p}") for p in range(2)]
        mask_done, neg_max_done, split_step = sem("mask_done"), sem("neg_max_done"), sem("split_step")
        xq_loaded, q_hi_done, q_mid_done, q_done = sem("xq_loaded"), sem("q_hi_done"), sem("q_mid_done"), sem("q_done")
        row_full, row_done = sem("row_full"), sem("row_done")
        score_full, probs_done, pv_done, attn_ready = (sem("score_full"), sem("probs_done"), sem("pv_done"),
                                                       sem("attn_ready"))
        aux_full, aux_free = sem("aux_full"), sem("aux_free")
        rstd_done = sem("rstd_done")
        norm_done, x_res_in, ln2_step, out_stored = sem("norm_done"), sem("x_res_in"), sem("ln2_step"), sem("out_stored")

        passed = {e.engine: sem(f"passed_{n}") for n, e in (("pool", nc.gpsimd), ("act", nc.scalar), ("dve", nc.vector))}
        LN_STEPS = 3 * SUB + 2
        LN_STATS = 2 * SUB + 2

        def layer_norm_stats(wait_chain, chain, src):
            for s in range(SUB):
                nc.vector.bn_stats(stats[:, s, :], src[:, s, :]).then_inc(chain, 1)
            wait_chain(SUB)
            settled(nc.vector)
            for s in range(SUB):
                nc.vector.bn_aggr(mean_var[:, s, :], stats[:, s, :]).then_inc(chain, 1)
            wait_chain(2 * SUB)
            nc.vector.tensor_scalar(inv_var[:, :], mean_var[:, :, 1], EPS, None, ALU.add).then_inc(chain, 1)
            wait_chain(2 * SUB + 1)
            nc.vector.reciprocal(inv_var[:, :], inv_var[:, :]).then_inc(chain, 1)

        def layer_norm_apply(chain, src, dst):
            for s in range(SUB):
                nc.vector.tensor_scalar(dst[:, s, :], src[:, s, :], mean_var[:, s, 0:1], rstd[:, s:s + 1],
                                        ALU.subtract, ALU.mult).then_inc(chain, 1)

        def settled(eng):
            eng.sem_inc(passed[eng.engine], 1)

        block = ctx.enter_context(nc.Block())

        @block.sync
        def _(sp):
            def load_adj(n, c, half):
                sp.dma_start(adj_in[:, half, :], adj[bass.ts(n, 128), c * ADJ_W:(c + 1) * ADJ_W])\
                  .then_inc(adj_loaded[half], 16)

            x_view = x.rearrange("(t p) d -> p t d", p=128)
            sp.dma_start(x_all[:, 0:SUB, :], x_view[:, 0:SUB, :]).then_inc(x_first, 16)
            load_adj(0, 0, 0)
            sp.dma_start(wqkv, w_qkv).then_inc(w_in, 16)
            sp.dma_start(ident[:, :], const[:, 0:128]).then_inc(consts_in, 16)
            sp.dma_start(sum_sel[:, :], const[:, 128:256]).then_inc(consts_in, 16)
            sp.dma_start(part_coef[:, :], const[:, 256:260]).then_inc(consts_in, 16)
            with nc.allow_non_contiguous_dma(reason="small vectors onto partitions"):
                for n, v in enumerate((g1, be1, g2, be2)):
                    sp.dma_start(gb[:, n:n + 1], v.rearrange("(p a) -> p a", a=1)).then_inc(consts_in, 16)
                sp.dma_start(b1_col[:, :], b1.rearrange("(f p) -> p f", p=128)).then_inc(consts_in, 16)
            sp.dma_start(x_all[:, SUB:, :], x_view[:, SUB:, :]).then_inc(x_in, 16)

            load_adj(1, 0, 1)
            for k in range(2, 4):
                sp.wait_ge(mask_done, k - 1)
                load_adj(k % SUB, k // SUB, k % 2)
            sp.wait_ge(wp_clear, 1)
            for h in range(HEADS):
                r = 32 * (h % 4)
                sp.dma_start(wp_pad[r:r + HD, h // 4, :], w_proj[h * HD:(h + 1) * HD, :]).then_inc(wp_in, 16)
            sp.dma_start(wp_pad[HD:HD + 1, 0, :], b_proj.rearrange("(a d) -> a d", a=1)).then_inc(wp_in, 16)
            sp.dma_start(w1_sb[:, :], w1).then_inc(wp_in, 16)
            sp.dma_start(w2_sb[:, :, :], w2.rearrange("(f p) d -> p f d", p=128)).then_inc(wp_in, 16)
            sp.dma_start(b2_row[:, :], b2.rearrange("(a d) -> a d", a=1)).then_inc(wp_in, 16)
            for k in range(4, SUB * ADJ_C):
                sp.wait_ge(mask_done, k - 1)
                load_adj(k % SUB, k // SUB, k % 2)
            with sp.Fori(SUB, SUBS) as n:
                for c in range(ADJ_C):
                    sp.wait_ge(mask_done, n * ADJ_C + (c - 1))
                    load_adj(n, c, c % 2)

        @block.gpsimd
        def _(pool):
            nc.gpsimd.memset(wp_pad[:, :, :], 0.0).then_inc(wp_clear, 1)
            nc.gpsimd.memset(ones_row[:, :], 1.0).then_inc(set_up, 1)
            nc.gpsimd.memset(v_ones[:, :, :, HD:HD + 1], 1.0).then_inc(k_ones, 1)
            two_ones = float(np.array([0x3F803F80], np.uint32).view(np.float32)[0])

            def convert(target, c, half, times):
                pool.wait_ge(adj_loaded[half], 16 * times)
                settled(pool)
                nc.gpsimd.tensor_scalar(target[:, c * ADJ_W:(c + 1) * ADJ_W], adj_in[:, half, :],
                                        0.0, -BIG, ALU.is_equal, ALU.mult).then_inc(mask_done, 1)

            def split(full, rest, part, start):
                nc.gpsimd.tensor_copy(part[0], full).then_inc(split_step, 1)
                pool.wait_ge(split_step, start + 1)
                settled(pool)
                nc.gpsimd.tensor_tensor(rest, full, part[0], ALU.subtract).then_inc(split_step, 1)
                pool.wait_ge(split_step, start + 2)
                settled(pool)
                nc.gpsimd.tensor_copy(part[1], rest).then_inc(split_step, 1)
                pool.wait_ge(split_step, start + 3)
                settled(pool)
                nc.gpsimd.tensor_tensor(rest, rest, part[1], ALU.subtract).then_inc(split_step, 1)
                pool.wait_ge(split_step, start + 4)
                settled(pool)
                nc.gpsimd.tensor_copy(part[2], rest).then_inc(split_step, 1)

            def split_first():
                pool.wait_ge(neg_max_done, SUB)
                split(neg_max[:, :, :], max_rest[:, :, :], [max_part[:, :, :, k] for k in range(3)], 0)

            def split_max(n, place):
                pool.wait_ge(neg_max_done, n + 1)
                settled(pool)
                split(neg_max[:, place, :], max_rest[:, place, :], [max_part[:, place, :, k] for k in range(3)],
                      n * SPLIT_OPS - (SUB - 1) * SPLIT_OPS)

            for n in range(ITEMS):
                blk, h = n // HEADS, n % HEADS
                dst = q_stack[0][0:STACK, h, :] if blk == 0 else k_stack[0:STACK, h, 512 * (blk - 1):512 * blk]
                pool.wait_ge(mid_done, n + 1)
                nc.gpsimd.tensor_tensor(dst, item_rest[n % DEPTH], item_mid[n % DEPTH], ALU.add).then_inc(item_done, 1)
                if n in POOL_FIRST_MASKS:
                    k = POOL_FIRST_MASKS[n]
                    if k == 4:
                        pool.wait_ge(mask_done, 4)
                    convert(first_mask[k % SUB], k // SUB, k % 2, k // 2 + 1)
                if n in POOL_NEXT_MASKS:
                    f = POOL_NEXT_MASKS[n]
                    pool.wait_ge(row_done, (2 * f + 2) * HEADS * SUB)
                    convert(row_mask[:, 0, :], f, f % 2, SUB * ADJ_C // 2 + f // 2 + 1)
                if n in POOL_ONES:
                    pool.wait_ge(item_done, n + 1)
                    nc.gpsimd.memset(k_stack[STACK:KROWS, POOL_ONES[n], :].bitcast(F32), two_ones).then_inc(k_ones, 1)
                    pool.wait_ge(k_ones, 2 + POOL_ONES[n])
            split_first()
            convert(row_mask[:, 0, :], ADJ_C - 1, (ADJ_C - 1) % 2, SUB * ADJ_C // 2 + (ADJ_C - 1) // 2 + 1)

            def mask_probs(i, par, g):
                for q in range(2):
                    pool.wait_ge(exps_bounded, i * NP + (POOL_PAIRS[g, q] + 1))
                    view = probs[:, slot(g, q), :].rearrange("p (a n) -> p a n", a=PAIR)
                    keep = mask_t[par][:, g % MB, :].unsqueeze(1).broadcast_to([128, PAIR, TILE])
                    settled(pool)
                    nc.gpsimd.tensor_tensor(view, view, keep, ALU.mult).then_inc(probs_masked, 1)

            def convert_next(i, j, f):
                if f == 0:
                    pool.wait_ge(neg_max_done, (i + 1) * SUB + (j - 1))
                convert(row_mask[:, j % 2, :], f, f % 2,
                        (i + 1) * (SUB * ADJ_C // 2) + (j * (ADJ_C // 2) + f // 2 + 1))

            def body(i, par, b, c, d):
                for g in range(GROUPS):
                    if b and g >= 1 and pool_masked((g - 1) % MB):
                        mask_probs(i, par, g - 1)
                    if b and g in SPLIT:
                        split_max((i + 1) * SUB + SPLIT[g], SPLIT[g] % 2)
                    if b and g in CONVERT and not (isinstance(i, int) and i == TILES - 2 and CONVERT[g][0] == SUB):
                        convert_next(i, *CONVERT[g])

            run_iterations(pool, body, (TILES - 4) // 2)

        @block.scalar
        def _(act):
            def store_mask(dest, f, j):
                src, dst = aux_bf.rearrange("p (m n) -> p m n", m=8), dest[:, 8 * f:8 * f + 8, 128 * j:128 * (j + 1)]
                theirs = [a for a in range(2) if pool_masked(8 * f + 4 * a + 3)]
                assert sum(pool_masked(8 * f + m) for m in range(8)) == len(theirs)
                settled(act)

                def store(mine, a, b, pool):
                    view = [v[:, 4 * mine[0]:4 * mine[-1] + 4, :].rearrange("p (h m) n -> p h m n", m=4)[:, :, a:b, :]
                            for v in (dst, src)]
                    return nc.scalar.activation(*view, ACT.Copy, scale=(1.0 if pool else -1.0) / BIG,
                                                bias=1.0 if pool else 0.0, saturate=False)

                if len(theirs) == 2:
                    store([0, 1], 0, 3, False)
                    last = store([0, 1], 3, 4, True)
                else:
                    ours = [m for m in range(8) if not pool_masked(8 * f + m)]
                    last = nc.scalar.activation(dst[:, 0:8, :], src[:, 0:8, :], ACT.Copy, scale=-1.0 / BIG,
                                                saturate=False) if not theirs else None
                    if theirs == [1]:
                        nc.scalar.activation(dst[:, 0:7, :], src[:, 0:7, :], ACT.Copy, scale=-1.0 / BIG,
                                             saturate=False)
                        last = store([1], 3, 4, True)
                    elif theirs == [0]:
                        store([0], 0, 3, False)
                        store([1], 0, 4, False)
                        last = store([0], 3, 4, True)
                last.then_inc(aux_free, 1)

            def store_shift(dest, bank, j):
                return nc.scalar.copy(dest[STACK:KROWS, :, 128 * j:128 * (j + 1)],
                                      bank.bitcast(BF16)[STACK:KROWS, :].rearrange("p (h n) -> p h n", h=HEADS))

            def root(c):
                act.wait_ge(ln1_step, c * LN_STEPS + LN_STATS)
                nc.scalar.activation(rstd[:, :], inv_var[:, :], ACT.Sqrt).then_inc(rstd_done, 1)

            def transposed_rows(c):
                act.wait_ge(stage_full, 2 * c + 1)
                if c >= 2:
                    act.wait_ge(xnT_stored[c % 2], 16 * (c // 2))
                nc.scalar.activation(xnT[c % 2], pv_ps[:, :], ACT.Identity, scale=gb[:, 0:1],
                                     bias=gb[:, 1:2]).then_inc(xnT_ready, 1)
                act.wait_ge(xnT_ready, c + 1)
                act.dma_start(xnT_dram[c if c > 0 else TILES], xnT[c % 2]).then_inc(xnT_stored[c % 2], 16)

            root(0)
            act.wait_ge(consts_in, 16 * 8)
            act.wait_ge(k_ones, 1)
            transposed_rows(0)
            for st in range(FIRST_STEPS):
                c, k = st // HEADS, st % HEADS
                if k == 0 and 1 <= c < CHUNKS:
                    transposed_rows(c)
                if st < ITEMS:
                    act.wait_ge(item_full, st + 1)
                    if st >= 2:
                        act.wait_ge(rest_done, st - 1)
                    col = 0 if st < HEADS else 2
                    nc.scalar.activation(item_hi[st % 2], score_ps[0:STACK, st % 4, :], ACT.Identity,
                                         scale=part_coef[0:STACK, col:col + 1]).then_inc(hi_done, 1)
                if 2 <= st <= ITEMS + 1:
                    n = st - 2
                    col = 1 if n < HEADS else 3
                    act.wait_ge(rest_done, n + 1)
                    if n >= DEPTH:
                        act.wait_ge(item_done, n - DEPTH + 1)
                    nc.scalar.activation(item_mid[n % DEPTH], item_rest[n % DEPTH], ACT.Identity,
                                         scale=part_coef[0:STACK, col:col + 1]).then_inc(mid_done, 1)
                if k == 4 and c < CHUNKS:
                    act.wait_ge(stage_full, 2 * c + 2)
                    nc.scalar.copy(v_ones[:, c * SUB:(c + 1) * SUB, :, 0:HD],
                                   pv_ps[:, :].rearrange("p (s h d) -> p s h d", s=SUB, h=HEADS)).then_inc(v_done, 1)
                if k == 5 and c + 1 < CHUNKS:
                    root(c + 1)
                if st in FIRST_MASKS:
                    n = FIRST_MASKS[st]
                    act.wait_ge(aux_full, n + 1)
                    store_mask(mask_t[0], n // SUB, n % SUB)
            for j in range(SUB):
                act.wait_ge(shift_full, j + 1)
                store_shift(q_stack[0], score_ps[:, j, :], j).then_inc(shift_stored, 1)
            act.wait_ge(xnT_stored[0], 16 * (TILES // 2))
            act.wait_ge(xnT_stored[1], 16 * (TILES // 2))
            act.dma_start(xq[:, :], xnT_dram[1]).then_inc(xq_loaded, 16)

            x_view = x.rearrange("(t s p) d -> t p s d", p=128, s=SUB)
            out_view = out.rearrange("(t s p) d -> t p s d", p=128, s=SUB)

            def tile_of(view, t):
                return view[t] if isinstance(t, int) else view[bass.ds(t, 1)].rearrange("a p s d -> p (a s) d")

            def exp_bounded(i, g, q):
                act.wait_ge(scores_bounded, i * NP + (POOL_PAIRS[g, q] + 1))
                nc.scalar.activation(probs[:, slot(g, q), :], probs[:, slot(g, q), :], ACT.Exp,
                                     scale=-1.0).then_inc(exps_bounded, 1)

            def body(i, par, b, c, d):
                nxt = 1 - par
                base = fills_before(i)
                plan = fill_plan(b, c, d)
                for g in range(GROUPS):
                    if g == 0:
                        act.wait_ge(aux_free, base)
                        if d:
                            act.dma_start(x_res[:, :, :], tile_of(x_view, i - 1)).then_inc(x_res_in, 16)
                    if b and g == XQ_STEP:
                        src = xnT_dram[i + 2] if isinstance(i, int) else \
                            xnT_dram[bass.ds(i + 2, 1)].rearrange("a p n -> p (a n)")
                        act.dma_start(xq[:, :], src).then_inc(xq_loaded, 16)
                    if b and 2 <= g <= HEADS + 1:
                        act.wait_ge(aux_free, base + plan[g - 2][0] + 1)
                        nc.scalar.copy(q_mid[:, :], q_rest[:, :]).then_inc(q_mid_done, 1)
                    pos, what = plan.get(g - 1, (0, (None,)))
                    if what[0] in ("q", "mask", "shift", "h2t", "up"):
                        act.wait_ge(aux_full, base + pos + 1)
                    if what[0] == "q":
                        nc.scalar.copy(q_hi[:, :], aux_ps[0:STACK, :]).then_inc(q_hi_done, 1)
                    elif what[0] == "mask":
                        store_mask(mask_t[nxt], what[2], what[1])
                    elif what[0] == "shift":
                        store_shift(q_stack[nxt], aux_ps[:, :], what[1]).then_inc(aux_free, 1)
                    elif what[0] == "h2t":
                        nc.scalar.activation(h2T[:, :], aux_ps[:, :], ACT.Identity, scale=gb[:, 2:3],
                                             bias=gb[:, 3:4]).then_inc(aux_free, 1)
                    elif what[0] == "up" and not c:
                        nc.scalar.activation(hidden[:, what[1], :], score_ps[:, what[1], :], ACT.Gelu_apprx_tanh,
                                             bias=b1_col[:, what[1]:what[1] + 1]).then_inc(aux_free, 1)
                    elif what[0] == "up":
                        nc.scalar.activation(hidden[:, what[1], :], aux_ps[:, :], ACT.Identity,
                                             bias=b1_col[:, what[1]:what[1] + 1]).then_inc(aux_free, 1)
                    if d and g == LAG:
                        act.wait_ge(pv_done, i * GROUPS)
                        nc.scalar.copy(attn[:, 1, :], pv_ps[:, :]).then_inc(attn_ready, 1)
                    if c and g == MB + LAG:
                        act.wait_ge(pv_done, i * GROUPS + MB)
                        nc.scalar.copy(attn[:, 0, :], pv_ps[:, :]).then_inc(attn_ready, 1)
                    if c:
                        for q in range(2):
                            if last_user(g, q) >= 0 or not (isinstance(i, int) and i == 0):
                                act.wait_ge(pv_done, i * GROUPS + (last_user(g, q) + 1))
                            n = 2 * g + q
                            act.wait_ge(score_full, i * EXPS + (n + 1))
                            scores = score_ps[:, 2 * q:2 * q + 2, :].rearrange("p a n -> p (a n)")
                            if pool_masked(g % MB) and not b:
                                act.wait_ge(scores_bounded, i * NP + (POOL_PAIRS[g, q] + 1))
                                nc.scalar.activation(probs[:, slot(g, q), :], probs[:, slot(g, q), :], ACT.Exp)\
                                  .then_inc(exps_bounded, 1)
                            elif pool_masked(g % MB):
                                nc.scalar.activation(probs[:, slot(g, q), :], scores, ACT.Relu, scale=-1.0)\
                                  .then_inc(scores_bounded, 1)
                            else:
                                nc.scalar.activation(probs[:, slot(g, q), :], scores, ACT.Exp)\
                                  .then_inc(probs_done, 1)
                                if b and g > 0 and q == 0 and pool_masked((g - 1) % MB):
                                    exp_bounded(i, g - 1, 1)
                        if b and pool_masked(g % MB):
                            exp_bounded(i, g, 0)
                    if d and c and g == GELU_STEP:
                        act.wait_ge(aux_free, base + plan[25][0] + 1)
                        nc.scalar.activation(hidden[:, :, :].rearrange("p f n -> p (f n)"),
                                             hidden[:, :, :].rearrange("p f n -> p (f n)"),
                                             ACT.Gelu_apprx_tanh).then_inc(gelu_done, 1)
                    if d and g == SQRT_STEP:
                        act.wait_ge(ln2_step, (i - 1) * LN_STEPS + LN_STATS)
                        nc.scalar.activation(rstd[:, :], inv_var[:, :], ACT.Sqrt).then_inc(rstd_done, 1)
                    if d and g == STORE_STEP:
                        act.wait_ge(aux_free, base + plan[32][0] + 1)
                        act.dma_start(tile_of(out_view, i - 1), rows2[:, :, :]).then_inc(out_stored, 16)
                    if d and g == SEEN_STEP:
                        act.wait_ge(out_stored, i * 16)

            run_iterations(act, body)
            act.wait_ge(out_stored, 16 * TILES)

        @block.vector
        def _(dve):
            def stats1(c):
                if c == 1:
                    dve.wait_ge(x_in, 16)
                layer_norm_stats(lambda k: dve.wait_ge(ln1_step, c * LN_STEPS + k), ln1_step,
                                 x_all[:, c * SUB:(c + 1) * SUB, :])

            def apply1(c):
                dve.wait_ge(rstd_done, c + 1)
                if c >= 2:
                    dve.wait_ge(stage_full, 2 * (c - 2) + 1)
                layer_norm_apply(ln1_step, x_all[:, c * SUB:(c + 1) * SUB, :], xn_rows[c % 2])

            def row_maximum(total, j, h, ch, mask, slot):
                settled(dve)
                nc.vector.tensor_tensor_reduce(
                    out=masked_out[:, (total - 1) % 2, :], in0=row_ps[:, (total - 1) % 2, :],
                    in1=mask[:, ch * 512:(ch + 1) * 512], scale=1.0, scalar=-3.0e38,
                    op0=ALU.add, op1=ALU.max, accum_out=row_max[:, slot, h, ch:ch + 1]).then_inc(row_done, 1)

            def first_masks(k):
                dve.wait_ge(adj_loaded[k % 2], 16 * (k // 2 + 1))
                nc.vector.tensor_scalar(first_mask[k % SUB][:, 0:ADJ_W], adj_in[:, k % 2, :],
                                        0.0, -BIG, ALU.is_equal, ALU.mult).then_inc(mask_done, 1)

            dve.wait_ge(x_first, 16)
            stats1(0)
            first_masks(0)
            apply1(0)
            dve.wait_ge(w_in, 16)
            for r in range(len(Q_PART)):
                nc.vector.tensor_scalar(wq_rep[:, :, HD * r:HD * (r + 1)],
                                        wqkv[:, 0:DIM].rearrange("p (h d) -> p h d", d=HD), SCALE, None,
                                        ALU.mult).then_inc(w_rep, 1)
                nc.vector.tensor_copy(wk_rep[:, :, HD * r:HD * (r + 1)],
                                      wqkv[:, DIM:2 * DIM].rearrange("p (h d) -> p h d", d=HD)).then_inc(w_rep, 1)
            dve.wait_ge(consts_in, 16 * 8)
            nc.vector.tensor_copy(ident_bf[:, :], ident[:, :]).then_inc(w_rep, 1)
            nc.vector.tensor_scalar(neg_ident[:, :], ident[:, :], -BIG, None, ALU.mult).then_inc(w_rep, 1)
            first_masks(1)
            for st in range(FIRST_STEPS):
                blk, h = st // HEADS, st % HEADS
                if 1 <= st <= ITEMS:
                    n = st - 1
                    dve.wait_ge(hi_done, n + 1)
                    if n >= DEPTH:
                        dve.wait_ge(item_done, n - DEPTH + 1)
                    nc.vector.tensor_tensor(item_rest[n % DEPTH], score_ps[0:STACK, n % 4, :], item_hi[n % 2],
                                            ALU.add).then_inc(rest_done, 1)
                if st in DVE_MASKS:
                    first_masks(DVE_MASKS[st])
                rh, ch = first_rows(st)
                if rh is not None:
                    for j in range(SUB):
                        u = ch * (HEADS * SUB) + rh * SUB + j
                        dve.wait_ge(row_full, u + 1)
                        if rh == 0:
                            dve.wait_ge(mask_done, ch // 2 * SUB + j + 1)
                        row_maximum(u + 1, j, rh, ch, first_mask[j], j)
                if h == 1 and blk + 1 < CHUNKS:
                    stats1(blk + 1)
                if h == 6 and blk + 1 < CHUNKS:
                    apply1(blk + 1)
            dve.wait_ge(v_done, CHUNKS)
            nc.vector.memset(pv_ps[:, :], 0.0).then_inc(pv_clear, 1)
            dve.wait_ge(row_done, ROWS)
            nc.vector.tensor_reduce(neg_max[:, :, :], row_max[:, :, :, :], AX.X, ALU.max,
                                    negate=True).then_inc(neg_max_done, SUB)

            def maximum(i, u):
                j, h, ch = u // (HEADS * CHUNKS), u // CHUNKS % HEADS, u % CHUNKS
                if h == 0 and ch == 0:
                    dve.wait_ge(neg_max_done, (i + 1) * SUB + (j - 1))
                dve.wait_ge(row_full, (i + 1) * ROWS + (u + 1))
                if h == 0 and ch % 2 == 0:
                    dve.wait_ge(mask_done, (i + 1) * (SUB * ADJ_C) + (j * ADJ_C + ch // 2 + 1))
                row_maximum(u + 1, j, h, ch, row_mask[:, j % 2, :], j % 2)
                if u % (HEADS * CHUNKS) == HEADS * CHUNKS - 1:
                    dve.wait_ge(split_step, SPLIT_OPS * (1 + i * SUB + (j - 1)))
                    dve.wait_ge(row_done, (i + 1) * ROWS + (u + 1))
                    nc.vector.tensor_reduce(neg_max[:, j % 2, :], row_max[:, j % 2, :, :], AX.X, ALU.max,
                                            negate=True).then_inc(neg_max_done, 1)

            def bound_last_scores(i, g):
                for q in range(2):
                    dve.wait_ge(score_full, i * EXPS + (2 * g + q + 1))
                    dve.wait_ge(pv_done, i * GROUPS + (last_user(g, q) + 1))
                    nc.vector.tensor_scalar(probs[:, slot(g, q), :],
                                            score_ps[:, 2 * q:2 * q + 2, :].rearrange("p a n -> p (a n)"),
                                            0.0, None, ALU.min).then_inc(scores_bounded, 1)

            def mask_last_probs(i, par, g):
                for q in range(2):
                    dve.wait_ge(exps_bounded, i * NP + (POOL_PAIRS[g, q] + 1))
                    view = probs[:, slot(g, q), :].rearrange("p (a n) -> p a n", a=PAIR)
                    keep = mask_t[par][:, g % MB, :].unsqueeze(1).broadcast_to([128, PAIR, TILE])
                    nc.vector.tensor_tensor(view, view, keep, ALU.mult).then_inc(probs_masked, 1)

            def body(i, par, b, c, d):
                nxt = 1 - par
                base = fills_before(i)
                plan = fill_plan(b, c, d)
                for g in range(GROUPS):
                    rows = row_units(g) if b else []
                    ahead = 1 if b and 1 <= g <= HEADS + 1 else 2
                    for u in rows[0:ahead]:
                        maximum(i, u)
                    if c and not b and g >= 1 and pool_masked((g - 1) % MB):
                        mask_last_probs(i, par, g - 1)
                    if c and not b and pool_masked(g % MB):
                        bound_last_scores(i, g)
                    if b and 2 <= g <= HEADS + 1:
                        h = g - 2
                        dve.wait_ge(q_mid_done, i * HEADS + (h + 1))
                        if h == 0 and not (isinstance(i, int) and i == 0):
                            dve.wait_ge(probs_done, i * NO)
                        nc.vector.scalar_tensor_tensor(q_stack[nxt][0:STACK, h, :], q_mid[:, :],
                                                       part_coef[0:STACK, 1:2], q_rest[:, :], ALU.mult,
                                                       ALU.add).then_inc(q_done, 1)
                    pos, what = plan.get(g - 1, (0, (None,)))
                    if what[0] == "q":
                        dve.wait_ge(q_hi_done, i * HEADS + (what[1] + 1))
                        dve.wait_ge(q_done, i * HEADS + what[1])
                        nc.vector.scalar_tensor_tensor(q_rest[:, :], q_hi[:, :], part_coef[0:STACK, 0:1],
                                                       aux_ps[0:STACK, :], ALU.mult, ALU.add).then_inc(aux_free, 1)
                    elif what[0] == "sum":
                        dve.wait_ge(aux_full, base + pos + 1)
                        if not (isinstance(i, int) and i == 0):
                            dve.wait_ge(norm_done, i * HG - what[1])
                        nc.vector.reciprocal(recip[:, :], aux_ps[:, :]).then_inc(aux_free, 1)
                        dve.wait_ge(aux_free, base + pos + 1)
                        nc.vector.tensor_tensor(attn[:, what[1], :], attn[:, what[1], :], recip[:, :], ALU.mult)\
                          .then_inc(norm_done, 1)
                    elif what[0] == "proj":
                        dve.wait_ge(aux_full, base + pos + 1)
                        dve.wait_ge(x_res_in, i * 16)
                        nc.vector.tensor_tensor(x_res[:, :, :].rearrange("p s d -> p (s d)"), aux_ps[:, :],
                                                x_res[:, :, :].rearrange("p s d -> p (s d)"), ALU.add)\
                          .then_inc(aux_free, 1)
                        dve.wait_ge(aux_free, base + pos + 1)
                        layer_norm_stats(lambda k: dve.wait_ge(ln2_step, (i - 1) * LN_STEPS + k), ln2_step, x_res)
                    elif what[0] == "down":
                        dve.wait_ge(aux_full, base + pos + 1)
                        nc.vector.tensor_tensor(rows2[:, :, :].rearrange("p s d -> p (s d)"), aux_ps[:, :],
                                                x_res[:, :, :].rearrange("p s d -> p (s d)"), ALU.add)\
                          .then_inc(aux_free, 1)
                    if d and g == SQRT_STEP + 1:
                        dve.wait_ge(rstd_done, TILES + i)
                        layer_norm_apply(ln2_step, x_res, rows2)
                    for u in rows[ahead:]:
                        maximum(i, u)

            run_iterations(dve, body)

        @block.tensor
        def _(pe):
            pe.wait_ge(consts_in, 16 * 8)
            pe.wait_ge(w_rep, 2 * len(Q_PART) + 2)

            def transpose_mask(mask, f):
                for m in range(8):
                    last = nc.tensor.transpose(aux_bf[:, 128 * m:128 * (m + 1)],
                                               mask[:, (8 * f + m) * 128:(8 * f + m + 1) * 128], ident_bf[:, :])
                last.then_inc(aux_full, 1)

            def transpose_shift(bank, slot):
                bank = bank.bitcast(BF16)
                for h in range(HEADS):
                    last = nc.tensor.transpose(bank[STACK:KROWS, 128 * h:128 * (h + 1)], max_part[:, slot, h, :],
                                               ident_bf[:, :])
                return last

            def transpose_rows(c):
                pe.wait_ge(ln1_step, (c + 1) * LN_STEPS)
                pe.wait_ge(v_done, c)
                for s in range(SUB):
                    last = nc.tensor.transpose(pv_ps[:, 128 * s:128 * (s + 1)], xn_rows[c % 2][:, s, :], ident[:, :])
                last.then_inc(stage_full, 1)

            def first_row_scores(h, ch):
                pe.wait_ge(item_done, HEADS * (ch + 1) + h + 1)
                for j in range(SUB):
                    u = ch * (HEADS * SUB) + h * SUB + j
                    if u >= 2:
                        pe.wait_ge(row_done, u - 1)
                    nc.tensor.matmul(row_ps[:, u % 2, :], q_stack[0][0:STACK, h, 128 * j:128 * (j + 1)],
                                     k_stack[0:STACK, h, ch * 512:(ch + 1) * 512], start=True, stop=True)\
                      .then_inc(row_full, 1)

            transpose_rows(0)
            for st in range(FIRST_STEPS):
                blk, h = st // HEADS, st % HEADS
                if h == 0 and 1 <= blk < CHUNKS:
                    transpose_rows(blk)
                if st < ITEMS:
                    chunk = max(blk - 1, 0)
                    pe.wait_ge(xnT_ready, chunk + 1)
                    if st >= 4:
                        pe.wait_ge(rest_done, st - 3)
                    nc.tensor.matmul(score_ps[0:STACK, st % 4, :], (wq_rep if blk == 0 else wk_rep)[:, h, :],
                                     xnT[chunk % 2], start=True, stop=True).then_inc(item_full, 1)
                if first_rows(st)[0] is not None:
                    first_row_scores(*first_rows(st))
                if h == 4 and blk < CHUNKS:
                    pe.wait_ge(xnT_ready, blk + 1)
                    for s in range(SUB):
                        last = nc.tensor.matmul(pv_ps[:, 128 * s:128 * (s + 1)],
                                                xnT[blk % 2][:, 128 * s:128 * (s + 1)], wqkv[:, 2 * DIM:3 * DIM],
                                                start=True, stop=True)
                    last.then_inc(stage_full, 1)
                if st in FIRST_MASKS:
                    n = FIRST_MASKS[st]
                    if n > 0:
                        pe.wait_ge(aux_free, n)
                    pe.wait_ge(mask_done, n + 1)
                    transpose_mask(first_mask[n % SUB], n // SUB)
            pe.wait_ge(split_step, SPLIT_OPS)
            for j in range(SUB):
                transpose_shift(score_ps[:, j, :], j).then_inc(shift_full, 1)
            pe.wait_ge(shift_stored, SUB)
            pe.wait_ge(k_ones, 1 + HEADS)
            pe.wait_ge(v_done, TILES)
            pe.wait_ge(pv_clear, 1)
            pe.wait_ge(wp_in, 16 * (3 + HEADS + 1))
            pe.wait_ge(set_up, 1)

            def row_scores(i, nxt, u):
                j, h, ch = u // (HEADS * CHUNKS), u // CHUNKS % HEADS, u % CHUNKS
                if j == 0 and ch == 0:
                    pe.wait_ge(q_done, i * HEADS + (h + 1))
                pe.wait_ge(row_done, (i + 1) * ROWS + (u - 1))
                nc.tensor.matmul(row_ps[:, u % 2, :], q_stack[nxt][0:STACK, h, 128 * j:128 * (j + 1)],
                                 k_stack[0:STACK, h, ch * 512:(ch + 1) * 512], start=True, stop=True)\
                  .then_inc(row_full, 1)

            def pair_scores(i, par, g, q, between):
                hg, m = g // MB, g % MB
                if g == 0:
                    if not (isinstance(i, int) and i == 0):
                        pe.wait_ge(probs_done, i * NO + (q - 1))
                elif pool_masked((g - 1) % MB):
                    pe.wait_ge(scores_bounded, i * NP + (POOL_PAIRS[g - 1, q] + 1))
                else:
                    pe.wait_ge(probs_done, i * NO + (OTHER_PAIRS[g - 1, q] + 1))
                if pool_masked(m):
                    for a in range(PAIR):
                        h = 4 * hg + PAIR * q + a
                        last = nc.tensor.matmul(score_ps[:, 2 * q + a, :], k_stack[:, h, 128 * m:128 * (m + 1)],
                                                q_stack[par][:, h, :], start=True, stop=True)
                    last.then_inc(score_full, 1)
                    between()
                else:
                    for a in range(PAIR):
                        h = 4 * hg + PAIR * q + a
                        nc.tensor.matmul(score_ps[:, 2 * q + a, :], k_stack[:, h, 128 * m:128 * (m + 1)],
                                         q_stack[par][:, h, :], start=True, stop=False)
                    between()
                    for a in range(PAIR):
                        last = nc.tensor.matmul(score_ps[:, 2 * q + a, :], neg_ident[:, :], mask_t[par][:, m, :],
                                                start=False, stop=True)
                    last.then_inc(score_full, 1)

            def weigh_values(i, g):
                hg, m = g // MB, g % MB
                if pool_masked(m):
                    pe.wait_ge(probs_masked, i * NP + (POOL_PAIRS[g, 1] + 1))
                else:
                    pe.wait_ge(probs_done, i * NO + (OTHER_PAIRS[g, 1] + 1))
                if m == 0 and not (isinstance(i, int) and i == 0 and hg == 0):
                    pe.wait_ge(attn_ready, i * HG + hg)
                for k in range(4):
                    last = nc.tensor.matmul(pv_ps[32 * k:32 * k + HD + 1, :], v_ones[:, m, 4 * hg + k, :],
                                            probs[:, slot(g, k // PAIR), (k % PAIR) * TILE:(k % PAIR + 1) * TILE],
                                            start=(m == 0), stop=(m == MB - 1))
                last.then_inc(pv_done, 1)

            def fill(i, nxt, base, pos, what, alone):
                if alone and what[0] == "up":
                    pe.wait_ge(aux_free, base + (pos - what[1]))
                else:
                    pe.wait_ge(aux_free, base + pos)
                if what[0] == "q":
                    if what[1] == 0:
                        pe.wait_ge(xq_loaded, (i + 1) * 16)
                    last = nc.tensor.matmul(aux_ps[0:STACK, :], wq_rep[:, what[1], :], xq[:, :], start=True, stop=True)
                elif what[0] == "mask":
                    _, j, f = what
                    pe.wait_ge(mask_done, (i + 1) * (SUB * ADJ_C) + (j * ADJ_C + f + 1))
                    return transpose_mask(row_mask[:, j % 2, :], f)
                elif what[0] == "shift":
                    j = what[1]
                    pe.wait_ge(split_step, SPLIT_OPS * (1 + i * SUB + (j + 1)))
                    last = transpose_shift(aux_ps[:, :], j % 2)
                elif what[0] == "sum":
                    pe.wait_ge(attn_ready, i * HG + (1 if what[1] == 0 else 0))
                    last = nc.tensor.matmul(aux_ps[:, :], sum_sel[:, :], attn[:, what[1], :], start=True, stop=True)
                elif what[0] == "proj":
                    pe.wait_ge(norm_done, i * HG)
                    for s in range(SUB):
                        for hg in range(HG):
                            last = nc.tensor.matmul(aux_ps[:, 128 * s:128 * (s + 1)], attn[:, hg, 128 * s:128 * (s + 1)],
                                                    wp_pad[:, hg, :], start=(hg == 0), stop=(hg == HG - 1))
                elif what[0] == "h2t":
                    pe.wait_ge(ln2_step, i * LN_STEPS)
                    for s in range(SUB):
                        last = nc.tensor.transpose(aux_ps[:, 128 * s:128 * (s + 1)], rows2[:, s, :], ident[:, :])
                elif what[0] == "up":
                    f = what[1]
                    bank = score_ps[:, f, :] if alone else aux_ps[:, :]
                    last = nc.tensor.matmul(bank, w1_sb[:, 128 * f:128 * (f + 1)], h2T[:, :], start=True, stop=True)
                elif what[0] == "down":
                    if not alone:
                        pe.wait_ge(gelu_done, i)
                    for s in range(SUB):
                        for f in range(FC):
                            nc.tensor.matmul(aux_ps[:, 128 * s:128 * (s + 1)], hidden[:, f, 128 * s:128 * (s + 1)],
                                             w2_sb[:, f, :], start=(f == 0), stop=False)
                        last = nc.tensor.matmul(aux_ps[:, 128 * s:128 * (s + 1)], ones_row[:, :], b2_row[:, :],
                                                start=False, stop=True)
                last.then_inc(aux_full, 1)

            def body(i, par, b, c, d):
                nxt = 1 - par
                base = fills_before(i)
                plan = fill_plan(b, c, d)
                if c:
                    pe.wait_ge(aux_free, base)
                for g in range(GROUPS):
                    rows = row_units(g) if b else []
                    second = 2 if len(rows) > 4 else 1
                    before_values = {3: 2, 4: 3}.get(len(rows), 4)

                    def row_run(a, b):
                        for u in rows[a:b]:
                            row_scores(i, nxt, u)

                    if c:
                        pair_scores(i, par, g, 0, lambda: row_run(0, 1))
                        row_run(1, second)
                        pair_scores(i, par, g, 1, lambda: row_run(second, second + 1))
                        row_run(second + 1, before_values)
                    else:
                        row_run(0, 4)
                    if g < LAG and d:
                        weigh_values(i - 1, GROUPS - LAG + g)
                    if g >= LAG and c:
                        weigh_values(i, g - LAG)
                    if c:
                        row_run(before_values, len(rows))
                    if g in plan:
                        fill(i, nxt, base, *plan[g], not c)

            run_iterations(pe, body)


def constants():
    c = np.zeros((128, 260), np.float32)
    c[:, 0:128] = np.eye(128)
    for col in range(128):
        c[32 * (col // 32) + HD, 128 + col] = 1.0
    for r in range(STACK):
        c[r, 256] = -1.0 if Q_PART[r // HD] >= 1 else 0.0
        c[r, 257] = -1.0 if Q_PART[r // HD] == 2 else 0.0
        c[r, 258] = -1.0 if K_PART[r // HD] >= 1 else 0.0
        c[r, 259] = -1.0 if K_PART[r // HD] == 2 else 0.0
    return c


def kernel(**inputs):
    import concourse.bacc as bacc
    from concourse.bass_utils import run_bass_kernel_spmd

    nc = bacc.Bacc("TRN2", target_bir_lowering=False, num_devices=1, dynamic_dma_scratch_size=1024)
    names = ["x", "adj"] + ["L0_gnn_" + n for n in
                            ("w_qkv", "w_proj", "b_proj", "w1", "b1", "w2", "b2", "g1", "be1", "g2", "be2")]
    arrays = {n: np.ascontiguousarray(inputs[n]) for n in names}
    arrays["const"] = constants()
    args = [nc.dram_tensor(n, a.shape, mybir.dt.from_np(a.dtype), kind="ExternalInput").ap()
            for n, a in arrays.items()]
    out = nc.dram_tensor("out", (N, DIM), F32, kind="ExternalOutput").ap()
    program(nc, *args, out)
    result = run_bass_kernel_spmd(nc, [arrays], core_ids=[0])
    return result.results[0]["out"]
```
